# Optimizing a Trainium2 kernel written in Bass

```python
import numpy as np
import jax
import jax.numpy as jnp

def _softmax(x, axis=-1):
    return jax.nn.softmax(x, axis=axis)

def _gelu(x):
    return jax.nn.gelu(x, approximate=True)

def _silu(x):
    return jax.nn.silu(x)

def _sigmoid(x):
    return jax.nn.sigmoid(x)

def _layernorm(x, axis=-1, eps=1e-05):
    m = jnp.mean(x, axis=axis, keepdims=True)
    v = jnp.var(x, axis=axis, keepdims=True)
    return (x - m) / jnp.sqrt(v + eps)

def _scatter_add(tgt, idx, src, axis=0):
    return tgt.at[idx].add(src)

def _segment_sum(src, seg, n):
    return jax.ops.segment_sum(src, seg, n)
kernel_name = 'mk_rec_standalone_d1_rec_r8_546657'

def setup_inputs(seed: int=0):
    np.random.seed(seed)
    _w = jnp.asarray

    def _rec_inputs():
        import jax
        import jax.numpy as jnp
        _rk = jax.random.key(seed)
        r_x = jax.random.randint(jax.random.fold_in(_rk, 1), (512, 6250), 0, 2, jnp.int32)
        return r_x
    r_x = _rec_inputs()

    def _L0_rec_setup():
        import jax, jax.numpy as jnp
        import numpy as np
        B, VOCAB, F = (512, 6250, 64)
        key = jax.random.key(seed)
        k1, k2 = jax.random.split(key, 2)
        x = jax.random.randint(k1, (B, VOCAB), 0, 2, dtype=jnp.int32)
        V = jax.random.normal(k2, (VOCAB, F), dtype=jnp.float32) * 0.05
        bias = jnp.zeros((VOCAB, 1), dtype=jnp.float32)
        g_bias = jnp.zeros((), dtype=jnp.float32)
        return {'x': x, 'V': V, 'bias': bias, 'g_bias': g_bias}
    _L0_rec_all = _L0_rec_setup()
    _L0_rec_in = {k: v for k, v in _L0_rec_all.items() if k in ('V', 'bias', 'g_bias')}
    del _L0_rec_all
    return {'r_x': r_x, 'L0_rec_V': _L0_rec_in['V'], 'L0_rec_bias': _L0_rec_in['bias'], 'L0_rec_g_bias': _L0_rec_in['g_bias']}

def reference(r_x, L0_rec_V, L0_rec_bias, L0_rec_g_bias):
    import jax
    import jax.numpy as jnp

    def _L0_rec_ref(x, V, bias, g_bias):
        import jax, jax.numpy as jnp
        import numpy as np
        B, VOCAB, F = (512, 6250, 64)
        xf = x.astype(V.dtype)
        xv = xf @ V
        sum_sq = jnp.sum(xv * xv, axis=-1)
        sq_sum = xf @ jnp.sum(V * V, axis=-1)
        second_order = 0.5 * (sum_sq - sq_sum)
        linear = g_bias + xf @ bias
        return linear + second_order[:, None]
    y = _L0_rec_ref(r_x, L0_rec_V, L0_rec_bias, L0_rec_g_bias)
    return y

_drawn_inputs = setup_inputs


def setup_inputs(seed=0):
    import zlib

    import numpy as np

    out = dict(_drawn_inputs(seed))
    spreads = {'L0_rec_bias': (0.0, 0.1)}
    factors = {}
    for name, (base, spread) in spreads.items():
        noise = np.random.default_rng([zlib.crc32(name.encode()), seed]).standard_normal(out[name].shape)
        drawn = base * np.exp(spread * noise) if base else spread * noise
        out[name] = jnp.asarray(drawn.astype(out[name].dtype))
    for name, factor in factors.items():
        out[name] = (out[name] * factor).astype(out[name].dtype)
    return out
```

```python
import concourse.bass as bass
from concourse import mybir
from contextlib import ExitStack


def factorization_machine(nc, x, V, bias, g_bias, out):
    fp32 = mybir.dt.float32
    i32 = mybir.dt.int32
    ALU = mybir.AluOpType
    ACT = mybir.ActivationFunctionType
    AX = mybir.AxisListType

    B, K = x.shape
    F = V.shape[1]
    P = 128
    S = 32
    NQ = P // S
    G = B // S
    NC = -(-K // P)
    Q = NC * S
    OVER = NQ * Q - K
    START = [i * Q for i in range(NQ - 1)] + [K - Q]
    JS = [7] * 6 + [4, 3]
    NT = len(JS)
    C0 = [sum(JS[:t]) for t in range(NT)]
    assert sum(JS) == NC and OVER < JS[0] * S
    E = F + 1

    ctx = ExitStack()
    with ctx:
        def sb(name, shape, dt):
            return ctx.enter_context(nc.sbuf_tensor(name, shape, dt))

        def sem(name):
            return ctx.enter_context(nc.semaphore(name))

        x_in = [sb(f"x_in{t}", [P, G, JS[t] * S], i32) for t in range(NT)]
        x_turned = [sb(f"x_turned{n}", [P, max(JS), B], i32) for n in range(2)]
        x_float = [sb(f"x_float{n}", [P, max(JS), B], fp32) for n in range(2)]
        v_in = sb("v_in", [P, NC, F], fp32)
        bias_in = sb("bias_in", [P, NC], fp32)
        v_sq = sb("v_sq", [P, NC, F], fp32)
        v_sum = sb("v_sum", [P, NC], fp32)
        weights = sb("weights", [P, NC, E], fp32)
        g_sb = sb("g_sb", [1, 1], fp32)
        squares = sb("squares", [E, B], fp32)
        combine = sb("combine", [E, 1], fp32)
        y_row = sb("y_row", [1, B], fp32)
        xv = ctx.enter_context(nc.psum_tensor("xv", [P, B], fp32))
        y_ps = ctx.enter_context(nc.psum_tensor("y_ps", [P, B], fp32))

        x_landed = [sem(f"x_landed{t}") for t in range(NT)]
        v_landed = [sem(f"v_landed{n}") for n in range(2)]
        g_landed = sem("g_landed")
        turned = sem("turned")
        floated = sem("floated")
        multiplied = sem("multiplied")
        squared = sem("squared")
        summed = sem("summed")
        weighed = sem("weighed")
        copied = sem("copied")
        const_set = sem("const_set")
        sq_done = sem("sq_done")
        y_done = sem("y_done")
        row_done = sem("row_done")
        out_done = sem("out_done")

        PARTS = [(0, C0[1]), (C0[1], NC)]

        def rows_of(i, t, src):
            lo = START[i] + C0[t] * S
            return src[lo:lo + JS[t] * S, :].rearrange("(c j) f -> c (j f)", c=S)

        block = ctx.enter_context(nc.Block())

        @block.sync
        def _(sp):
            for t in range(NT):
                for i in range(NQ):
                    lo = START[i] + C0[t] * S
                    sp.dma_start(x_in[t][S * i:S * i + S, :, :],
                                 x[:, lo:lo + JS[t] * S].rearrange("(r g) l -> r g l", g=G)
                                 ).then_inc(x_landed[t], 16)
            sp.wait_ge(row_done, 1)
            sp.dma_start(out.rearrange("b o -> o b"), y_row[:, :]).then_inc(out_done, 16)
            sp.wait_ge(out_done, 16)

        @block.scalar
        def _(act):
            for t in range(NT):
                for i in range(NQ):
                    act.dma_start(v_in[S * i:S * i + S, C0[t]:C0[t] + JS[t], :].rearrange("c j f -> c (j f)"),
                                  rows_of(i, t, V)).then_inc(v_landed[min(t, 1)], 16)
                    act.dma_start(bias_in[S * i:S * i + S, C0[t]:C0[t] + JS[t]],
                                  rows_of(i, t, bias)).then_inc(v_landed[min(t, 1)], 16)
            act.dma_start(g_sb[:, :], g_bias.rearrange("(a b) -> a b", b=1)).then_inc(g_landed, 16)

            for n, (a, b) in enumerate(PARTS):
                parts = 1 if n == 0 else NT - 1
                act.wait_ge(v_landed[n], 32 * NQ * parts)
                nc.scalar.activation(v_sq[:, a:b, :], v_in[:, a:b, :], ACT.Square).then_inc(squared, 1)
                nc.scalar.copy(weights[:, a:b, 0:F], v_in[:, a:b, :]).then_inc(copied, 1)
                for t in ([0] if n == 0 else range(1, NT)):
                    act.wait_ge(turned, t + 1)
                    if t >= 2:
                        act.wait_ge(multiplied, t - 1)
                    nc.scalar.copy(x_float[t % 2][:, 0:JS[t], :], x_turned[t % 2][:, 0:JS[t], :]).then_inc(floated, 1)
            act.wait_ge(multiplied, NT)
            nc.scalar.activation(squares[0:F, :], xv[0:F, :], ACT.Square).then_inc(sq_done, 1)
            nc.scalar.copy(squares[F:E, :], xv[F:E, :]).then_inc(sq_done, 1)

        @block.vector
        def _(dve):
            nc.vector.memset(combine[0:F, :], 0.5).then_inc(const_set, 1)
            nc.vector.memset(combine[F:E, :], 1.0).then_inc(const_set, 1)

            def weigh(n):
                a, b = PARTS[n]
                dve.wait_ge(squared, n + 1)
                nc.vector.tensor_reduce(v_sum[:, a:b], v_sq[:, a:b, :], AX.X, ALU.add).then_inc(summed, 1)
                dve.wait_ge(summed, n + 1)
                nc.vector.scalar_tensor_tensor(weights[:, a:b, F], v_sum[:, a:b], -0.5, bias_in[:, a:b],
                                               op0=ALU.mult, op1=ALU.add).then_inc(weighed, 1)
                if n == 0:
                    dve.wait_ge(copied, 1)
                    dve.wait_ge(weighed, 1)
                    full, rest = divmod(OVER, JS[0])
                    q3 = S * (NQ - 1)
                    nc.vector.memset(weights[q3:q3 + full, 0:JS[0], :], 0.0).then_inc(weighed, 1)
                    dve.wait_ge(weighed, 2)
                    nc.vector.memset(weights[q3:q3 + full + 1, 0:rest, :], 0.0).then_inc(weighed, 1)

            for t in range(NT):
                dve.wait_ge(x_landed[t], 16 * NQ)
                if t >= 2:
                    dve.wait_ge(floated, t - 1)
                nc.vector.transpose(x_turned[t % 2][:, 0:JS[t], :].rearrange("p j (g r) -> p j g r", g=G),
                                    x_in[t][:, :, :].rearrange("p g (c j) -> p j g c", j=JS[t])
                                    ).then_inc(turned, 1)
                if t < 2:
                    weigh(t)
            dve.wait_ge(y_done, 1)
            dve.wait_ge(g_landed, 16)
            nc.vector.tensor_scalar_add(y_row[0:1, :].rearrange("o (r g) -> o g r", g=G),
                                        y_ps[0:1, :].rearrange("o (g r) -> o g r", g=G),
                                        g_sb[0:1, 0:1]).then_inc(row_done, 1)

        @block.tensor
        def _(pe):
            for t in range(NT):
                if t < 2:
                    pe.wait_ge(copied, t + 1)
                    pe.wait_ge(weighed, 3 + t)
                pe.wait_ge(floated, t + 1)
                for j in range(JS[t]):
                    c = C0[t] + j
                    last = nc.tensor.matmul(xv[0:E, :], weights[:, c, :], x_float[t % 2][:, j, :],
                                            start=(c == 0), stop=(c == NC - 1))
                last.then_inc(multiplied, 1)
            pe.wait_ge(sq_done, 2)
            pe.wait_ge(const_set, 2)
            nc.tensor.matmul(y_ps[0:1, :], combine[:, :], squares[:, :], start=True, stop=True).then_inc(y_done, 1)


_INS = ['r_x', 'L0_rec_V', 'L0_rec_bias', 'L0_rec_g_bias']
_OUTS = [((512, 1), 'float32')]


def kernel(**inputs):
    import numpy as _np
    import concourse.bacc as _bacc
    from concourse import mybir as _mybir
    from concourse.bass_utils import run_bass_kernel_spmd as _run

    nc = _bacc.Bacc("TRN2", target_bir_lowering=False, num_devices=1)
    arrays, args = {}, []
    for name in _INS:
        a = _np.ascontiguousarray(inputs[name])
        arrays[f"in_{name}_dram"] = a
        args.append(nc.dram_tensor(f"in_{name}_dram", a.shape, _mybir.dt.from_np(a.dtype), kind="ExternalInput").ap())
    for i, (shape, dtype) in enumerate(_OUTS):
        dt = _mybir.dt.from_np(_np.dtype(dtype))
        args.append(nc.dram_tensor(f"out_{i}_dram", shape, dt, kind="ExternalOutput").ap())
    factorization_machine(nc, *args)
    r = _run(nc, [arrays], core_ids=[0])
    got = tuple(r.results[0][f"out_{i}_dram"] for i in range(len(_OUTS)))
    return got[0]
```

```python
import concourse.bass as bass
from concourse import mybir
from contextlib import ExitStack


def factorization_machine(nc, x, V, bias, g_bias, out):
    fp32 = mybir.dt.float32
    bf16 = mybir.dt.bfloat16
    fp8 = mybir.dt.float8e4
    i32 = mybir.dt.int32
    u32 = mybir.dt.uint32
    ALU = mybir.AluOpType
    ACT = mybir.ActivationFunctionType
    AX = mybir.AxisListType

    B, K = x.shape
    F = V.shape[1]
    P = 128
    S = 32
    QUAD = 4
    W = QUAD * S
    NQ = P // S
    G = B // S
    NC = -(-K // P)
    ND = NC // QUAD
    Q = NC * S
    OVER = NQ * Q - K
    START = [i * Q for i in range(NQ - 1)] + [K - Q]
    assert NC == QUAD * ND + 1 and OVER < S
    E = F + 1
    EP = E + 1

    DS = [1, 2, 2, 2, 2, 2, 1]
    NT = len(DS)
    D0 = [sum(DS[:t]) for t in range(NT)]
    assert sum(DS) == ND
    GROUPS = [(0, 1), (1, 3), (3, NT)]
    NG = len(GROUPS)
    GROUP_AT = {a: n for n, (a, b) in enumerate(GROUPS)}
    NB = 3
    TOP_BITS = 0xC0C0C0C0
    TOP_BITS_ODD = 0xC000C000
    PARTS = 3

    def quads(t0, t1):
        return D0[t0], (ND if t1 == NT else D0[t1])

    def chunks(t0, t1):
        d0, d1 = quads(t0, t1)
        return (1 + QUAD * d0 if t0 else 0), 1 + QUAD * d1

    ctx = ExitStack()
    with ctx:
        def sb(name, shape, dt):
            return ctx.enter_context(nc.sbuf_tensor(name, shape, dt))

        def ps(name):
            return ctx.enter_context(nc.psum_tensor(name, [P, B], fp32))

        def sem(name):
            return ctx.enter_context(nc.semaphore(name))

        x_in = sb("x_in", [P, G, Q], i32)
        x_cast = [sb(f"x_cast{n}", [P, G * max(DS) * S], u32) for n in range(NB)]
        x_turned = [sb(f"x_turned{n}", [P, max(DS), B], u32) for n in range(NB)]
        odd_cast = sb("odd_cast", [P, G, S], bf16)
        odd_turned = sb("odd_turned", [P, G, S], bf16)
        v_in = sb("v_in", [P, NC, F], fp32)
        most = max(b - a for a, b in (chunks(*tiles) for tiles in GROUPS))
        v_rest = sb("v_rest", [P, most, F], fp32)
        v_sq = sb("v_sq", [P, most, F], fp32)
        parts = [sb(f"part{k}", [P, NC, EP], bf16) for k in range(PARTS)]
        bias_in = sb("bias_in", [P, W], fp32)
        bias_turned = sb("bias_turned", [P, QUAD, S], fp32)
        bias_odd = sb("bias_odd", [P, S], fp32)
        w_sum = sb("w_sum", [P, NC], fp32)
        w_all = sb("w_all", [P, NC], fp32)
        w_rest = sb("w_rest", [P, NC], fp32)
        g_sb = sb("g_sb", [1, 1], fp32)
        squares = sb("squares", [E, B], fp32)
        combine = sb("combine", [E, 1], fp32)
        ones = sb("ones", [P, 1], fp32)
        y_row = sb("y_row", [1, B], fp32)
        SEEN = G * S
        seen = sb("seen", [P, SEEN + G * S // 2], u32)
        foreign = sb("foreign", [P, 1], fp32)
        general = sb("general", [1, 1], i32)
        gen_float = x_cast[0][:, 0:B].bitcast(fp32).rearrange("p (g c) -> p g c", g=G)
        gen_turned = x_turned[0][:, 0, :].bitcast(fp32)
        gen_weights = x_turned[1][:, 0, 0:E].bitcast(fp32)
        gen_sum = x_turned[1][0:E, 1, :].bitcast(fp32)
        xv_ps = ps("xv_ps")
        y_ps = ps("y_ps")
        foreign_ps = ps("foreign_ps")
        gen_ps = ps("gen_ps")

        x_landed = [sem(f"x_landed{t}") for t in range(NT)]
        v_landed = [sem(f"v_landed{n}") for n in range(NG)]
        bias_landed = sem("bias_landed")
        g_landed = sem("g_landed")
        bias_cleared = sem("bias_cleared")
        overlap_cleared = sem("overlap_cleared")
        consts_set = sem("consts_set")
        high_ready = sem("high_ready")
        v_squared = sem("v_squared")
        v_summed = sem("v_summed")
        v_split = sem("v_split")
        w_split = sem("w_split")
        rest_ready = sem("rest_ready")
        mid_ready = sem("mid_ready")
        dve_step = sem("dve_step")
        x_cast_ready = sem("x_cast_ready")
        x_turned_ready = sem("x_turned_ready")
        odd_turned_ready = sem("odd_turned_ready")
        bias_turned_ready = sem("bias_turned_ready")
        w_odd = sem("w_odd")
        seen_ready = sem("seen_ready")
        odd_seen = sem("odd_seen")
        masked = sem("masked")
        multiplied = sem("multiplied")
        squares_ready = sem("squares_ready")
        linear_ready = sem("linear_ready")
        y_ready = sem("y_ready")
        row_ready = sem("row_ready")
        foreign_ready = sem("foreign_ready")
        foreign_summed = sem("foreign_summed")
        general_ready = sem("general_ready")
        out_done = sem("out_done")
        gen_float_ready = sem("gen_float_ready")
        gen_turned_ready = sem("gen_turned_ready")
        gen_weights_ready = sem("gen_weights_ready")
        gen_multiplied = sem("gen_multiplied")
        gen_added = sem("gen_added")

        v_loads = [NQ + (2 if n == 0 else 0) for n in range(NG)]

        def cast_words(t):
            return x_cast[t % NB][:, 0:G * DS[t] * S].rearrange("p (g l) -> p g l", g=G)

        def load_v(queue, n):
            d0, d1 = quads(*GROUPS[n])
            for i in range(NQ):
                queue.dma_start(
                    v_in[S * i:S * i + S, 1 + QUAD * d0:1 + QUAD * d1, :].rearrange("c (d q) f -> c d (q f)", q=QUAD),
                    V[START[i] + S + d0 * W:START[i] + S + d1 * W, :].rearrange("(d c q) f -> c d (q f)", c=S, q=QUAD)
                ).then_inc(v_landed[n], 16)

        def load_x(queue, t):
            lo = S + D0[t] * W if t else 0
            hi = S + (D0[t] + DS[t]) * W
            for i in range(NQ):
                queue.dma_start(x_in[S * i:S * i + S, :, lo:hi],
                                x[:, START[i] + lo:START[i] + hi].rearrange("(r g) l -> r g l", g=G)
                                ).then_inc(x_landed[t], 16)

        def gen_steps(loop, step):
            with loop(0, ND) as d:
                for q in range(QUAD):
                    step(d * QUAD + q, x_in[:, :, bass.ds(d * W + S, W)].rearrange("p g (c q) -> p q g c", q=QUAD)[:, q],
                         d * QUAD + (q + 1))
            step(NC - 1, x_in[:, :, 0:S], 0)

        block = ctx.enter_context(nc.Block())

        @block.sync
        def _(sp):
            last_quarter = NQ - 1
            sp.dma_start(v_in[0:S * last_quarter, 0, :],
                         V[0:Q * last_quarter, :].rearrange("(i l) f -> i l f", l=Q)[:, 0:S, :]
                         ).then_inc(v_landed[0], 16)
            sp.dma_start(v_in[S * last_quarter:P, 0, :],
                         V[START[last_quarter]:START[last_quarter] + S, :]).then_inc(v_landed[0], 16)
            for t in range(NT):
                if t in GROUP_AT:
                    load_v(sp, GROUP_AT[t])
                load_x(sp, t)
            sp.wait_ge(row_ready, 1)
            sp.dma_start(out.rearrange("b o -> o b"), y_row[:, :]).then_inc(out_done, 16)
            sp.wait_ge(out_done, 16)
            sp.wait_ge(general_ready, 1)
            with sp.If(sp.value_load(general[0:1, 0:1], min_val=0, max_val=1) > 0):
                sp.wait_ge(row_ready, 2)
                sp.dma_start(out.rearrange("b o -> o b"), y_row[:, :]).then_inc(out_done, 16)
                sp.wait_ge(out_done, 32)

        @block.gpsimd
        def _(pool):
            nc.gpsimd.memset(bias_in[:, :], 0.0).then_inc(bias_cleared, 1)
            pool.wait_ge(bias_cleared, 1)
            pool.dma_start(bias_in[0:1, W - S:W], bias[0:S, :].rearrange("l o -> o l")).then_inc(bias_landed, 16)
            pool.dma_start(bias_in[1:1 + ND, :], bias[S:Q, :].rearrange("(d l) o -> d (l o)", l=W)
                           ).then_inc(bias_landed, 16)
            for i in range(1, NQ):
                pool.dma_start(bias_in[S * i:S * i + 1 + ND, :],
                               bias[START[i] + S - W:START[i] + Q, :].rearrange("(d l) o -> d (l o)", l=W)
                               ).then_inc(bias_landed, 16)
            pool.dma_start(g_sb[:, :], g_bias.rearrange("(a b) -> a b", b=1)).then_inc(g_landed, 16)
            last_quarter = S * (NQ - 1)
            pool.wait_ge(v_landed[0], 16 * v_loads[0])
            nc.gpsimd.memset(v_in[last_quarter:last_quarter + OVER, 0, :], 0.0).then_inc(overlap_cleared, 1)
            pool.wait_ge(bias_landed, 16 * (NQ + 1))
            pool.wait_ge(overlap_cleared, 1)
            nc.gpsimd.memset(bias_in[last_quarter:last_quarter + 1, W - S:W - S + OVER], 0.0
                             ).then_inc(overlap_cleared, 1)
            pool.wait_ge(overlap_cleared, 2)
            for n, (t0, t1) in enumerate(GROUPS):
                a, b = chunks(t0, t1)
                v, rest = v_in[:, a:b, :], v_rest[:, 0:b - a, :]
                high, mid, low = (part[:, a:b, 0:F] for part in parts)
                pool.wait_ge(high_ready, n + 1)
                nc.gpsimd.tensor_tensor(rest, v, high, ALU.subtract).then_inc(rest_ready, 1)
                pool.wait_ge(mid_ready, n + 1)
                nc.gpsimd.tensor_tensor(low, rest, mid, ALU.subtract).then_inc(v_split, 1)
                pool.wait_ge(v_split, n + 1)

        @block.scalar
        def _(act):
            for t in range(NT):
                if t in GROUP_AT:
                    n = GROUP_AT[t]
                    a, b = chunks(*GROUPS[n])
                    act.wait_ge(v_landed[n], 16 * v_loads[n])
                    act.wait_ge(overlap_cleared, 1)
                    nc.scalar.copy(parts[0][:, a:b, 0:F], v_in[:, a:b, :]).then_inc(high_ready, 1)
                    if n >= 1:
                        act.wait_ge(v_summed, n)
                    nc.scalar.activation(v_sq[:, 0:b - a, :], v_in[:, a:b, :], ACT.Square).then_inc(v_squared, 1)
                act.wait_ge(x_landed[t], 16 * NQ)
                if t >= NB:
                    act.wait_ge(seen_ready, D0[t - NB] + DS[t - NB])
                lo = S + D0[t] * W
                nc.scalar.copy(cast_words(t).bitcast(fp8), x_in[:, :, lo:lo + DS[t] * W],
                               saturate=False).then_inc(x_cast_ready, 1)

            def finish(n, source):
                nc.scalar.activation(squares[0:F, :], source[0:F, :], ACT.Square).then_inc(squares_ready, 1)

            act.wait_ge(multiplied, NT)
            finish(0, xv_ps)
            act.wait_ge(general_ready, 1)
            with act.If(act.value_load(general[0:1, 0:1], min_val=0, max_val=1) > 0):
                def step(n, entries, chunk):
                    act.wait_ge(gen_turned_ready, n + 1)
                    nc.scalar.copy(gen_float, entries).then_inc(gen_float_ready, 1)
                gen_steps(act.Fori, step)
                act.wait_ge(gen_added, NC + 1)
                act.wait_ge(y_ready, 1)
                finish(1, gen_sum)

        @block.vector
        def _(dve):
            steps = [0]

            def chained(instruction):
                steps[0] += 1
                instruction.then_inc(dve_step, 1)
                dve.wait_ge(dve_step, steps[0])

            nc.vector.memset(combine[0:F, :], 0.5).then_inc(consts_set, 1)
            nc.vector.memset(combine[F:E, :], 1.0).then_inc(consts_set, 1)
            nc.vector.memset(ones[:, :], 1.0).then_inc(consts_set, 1)

            def turn_odd():
                dve.wait_ge(x_landed[0], 16 * NQ)
                chained(nc.vector.tensor_copy(odd_cast[:, :, :], x_in[:, :, 0:S]))
                nc.vector.transpose(odd_turned[:, :, :], odd_cast[:, :, :]).then_inc(odd_turned_ready, 1)
                nc.vector.tensor_copy(seen[:, SEEN:], odd_cast[:, :, :].rearrange("p g l -> p (g l)").bitcast(u32)
                                      ).then_inc(odd_seen, 1)

            def turn(t):
                dve.wait_ge(x_cast_ready, t + 1)
                if t >= NB:
                    dve.wait_ge(multiplied, t - NB + 1)
                nc.vector.transpose(x_turned[t % NB][:, 0:DS[t], :].rearrange("p d (g r) -> p d g r", g=G),
                                    cast_words(t).rearrange("p g (d c) -> p d g c", c=S)).then_inc(x_turned_ready, 1)

            def check(t):
                for k in range(DS[t]):
                    words = x_cast[t % NB][:, k * SEEN:(k + 1) * SEEN]
                    before = D0[t] + k
                    if before == 0:
                        nc.vector.tensor_copy(seen[:, 0:SEEN], words).then_inc(seen_ready, 1)
                        continue
                    dve.wait_ge(seen_ready, before)
                    nc.vector.tensor_tensor(seen[:, 0:SEEN], seen[:, 0:SEEN], words,
                                            ALU.bitwise_or).then_inc(seen_ready, 1)

            def weigh(n):
                a, b = chunks(*GROUPS[n])
                d0, d1 = quads(*GROUPS[n])
                dve.wait_ge(v_squared, n + 1)
                nc.vector.tensor_reduce(w_sum[:, a:b], v_sq[:, 0:b - a, :], AX.X, ALU.add).then_inc(v_summed, 1)
                dve.wait_ge(v_summed, n + 1)
                if n == 0:
                    nc.vector.scalar_tensor_tensor(w_all[:, 0:1], w_sum[:, 0:1], -0.5, bias_odd[:, 0:1],
                                                   op0=ALU.mult, op1=ALU.add).then_inc(w_odd, 1)
                    dve.wait_ge(w_odd, 1)
                quad_sums = slice(1 + QUAD * d0, 1 + QUAD * d1)
                chained(nc.vector.scalar_tensor_tensor(
                    w_all[:, quad_sums].rearrange("p (d q) -> p d q", q=QUAD),
                    w_sum[:, quad_sums].rearrange("p (d q) -> p d q", q=QUAD), -0.5,
                    bias_turned[:, :, 1 + d0:1 + d1].rearrange("p q d -> p d q"),
                    op0=ALU.mult, op1=ALU.add))
                high, mid, low = (part[:, a:b, F] for part in parts)
                chained(nc.vector.tensor_copy(high, w_all[:, a:b]))
                chained(nc.vector.tensor_tensor(w_rest[:, a:b], w_all[:, a:b], high, ALU.subtract))
                chained(nc.vector.tensor_copy(mid, w_rest[:, a:b]))
                nc.vector.tensor_tensor(low, w_rest[:, a:b], mid, ALU.subtract).then_inc(w_split, 1)

            def middle(n):
                a, b = chunks(*GROUPS[n])
                dve.wait_ge(rest_ready, n + 1)
                nc.vector.tensor_copy(parts[1][:, a:b, 0:F], v_rest[:, 0:b - a, :]).then_inc(mid_ready, 1)

            turn_odd()
            middle(0)
            turn(0)
            dve.wait_ge(bias_landed, 16 * (NQ + 1))
            dve.wait_ge(overlap_cleared, 2)
            nc.vector.transpose(bias_odd[:, :], bias_in[:, W - S:W]).then_inc(bias_turned_ready, 1)
            nc.vector.transpose(bias_turned[:, :, :], bias_in[:, :].rearrange("p (c q) -> p q c", q=QUAD)
                                ).then_inc(bias_turned_ready, 1)
            dve.wait_ge(bias_turned_ready, 2)
            weigh(0)
            check(0)
            for t in range(1, NT):
                turn(t)
                if t in GROUP_AT:
                    middle(GROUP_AT[t])
                    weigh(GROUP_AT[t])
                check(t)

            dve.wait_ge(multiplied, NT)
            nc.vector.tensor_copy(squares[F:E, :], xv_ps[F:E, :]).then_inc(linear_ready, 1)
            dve.wait_ge(seen_ready, ND)
            dve.wait_ge(odd_seen, 1)
            for words, mask in ((seen[:, 0:SEEN], TOP_BITS), (seen[:, SEEN:], TOP_BITS_ODD)):
                nc.vector.tensor_scalar(words, words, mask, None, ALU.bitwise_and).then_inc(masked, 1)
            dve.wait_ge(masked, 2)
            nc.vector.tensor_reduce(foreign[:, :], seen[:, :], AX.X, ALU.max).then_inc(foreign_ready, 1)
            dve.wait_ge(foreign_summed, 1)
            nc.vector.tensor_scalar(general[0:1, 0:1], foreign_ps[0:1, 0:1], 0.0, None, ALU.is_gt).then_inc(general_ready, 1)

            def finish(n):
                dve.wait_ge(y_ready, n + 1)
                nc.vector.tensor_scalar_add(y_row[0:1, :].rearrange("o (r g) -> o g r", g=G),
                                            y_ps[0:1, :].rearrange("o (g r) -> o g r", g=G),
                                            g_sb[0:1, 0:1]).then_inc(row_ready, 1)

            dve.wait_ge(g_landed, 16)
            finish(0)
            dve.wait_ge(general_ready, 1)
            with dve.If(dve.value_load(general[0:1, 0:1], min_val=0, max_val=1) > 0):
                dve.sem_inc(gen_turned_ready, 1)
                nc.vector.memset(gen_sum, 0.0).then_inc(gen_added, 1)
                dve.wait_ge(gen_added, 1)

                def step(n, entries, chunk):
                    dve.wait_ge(gen_float_ready, n + 1)
                    nc.vector.transpose(gen_turned.rearrange("p (g r) -> p g r", g=G),
                                        gen_float).then_inc(gen_turned_ready, 1)
                    nc.vector.tensor_copy(gen_weights[:, 0:F], v_in[:, bass.ds(chunk, 1), :].rearrange("p n f -> p (n f)")
                                          ).then_inc(gen_weights_ready, 1)
                    nc.vector.tensor_copy(gen_weights[:, F:E], w_all[:, bass.ds(chunk, 1)]).then_inc(gen_weights_ready, 1)
                    dve.wait_ge(gen_multiplied, n + 1)
                    nc.vector.tensor_tensor(gen_sum, gen_sum, gen_ps[0:E, :], ALU.add
                                            ).then_inc(gen_added, 1)
                    dve.wait_ge(gen_added, n + 2)
                gen_steps(dve.Fori, step)
                nc.vector.tensor_copy(squares[F:E, :], gen_sum[F:E, :]).then_inc(linear_ready, 1)
                dve.wait_ge(out_done, 16)
                finish(1)

        @block.tensor
        def _(pe):
            for t in range(NT):
                if t in GROUP_AT:
                    pe.wait_ge(v_split, GROUP_AT[t] + 1)
                    pe.wait_ge(w_split, GROUP_AT[t] + 1)
                pe.wait_ge(x_turned_ready, t + 1)
                entries = x_turned[t % NB][:, :, :].bitcast(fp8).rearrange("p d (b q) -> p d q b", q=QUAD)
                moving = [entries[:, d, q, :] for d in range(DS[t]) for q in range(QUAD)]
                if t == 0:
                    pe.wait_ge(odd_turned_ready, 1)
                    moving.insert(0, odd_turned[:, :, :].rearrange("p g r -> p (g r)"))
                for n, column in enumerate(moving, chunks(t, t + 1)[0]):
                    for k in range(PARTS):
                        last = nc.tensor.matmul(xv_ps[0:E, :], parts[k][:, n, 0:E], column,
                                                start=(n == 0 and k == 0), stop=(n == NC - 1 and k == PARTS - 1))
                last.then_inc(multiplied, 1)

            def finish(n):
                pe.wait_ge(squares_ready, n + 1)
                pe.wait_ge(linear_ready, n + 1)
                nc.tensor.matmul(y_ps[0:1, :], combine[:, :], squares[:, :], start=True, stop=True).then_inc(y_ready, 1)

            pe.wait_ge(consts_set, 3)
            finish(0)
            pe.wait_ge(foreign_ready, 1)
            nc.tensor.matmul(foreign_ps[0:1, 0:1], foreign[:, :], ones[:, :], start=True, stop=True).then_inc(foreign_summed, 1)
            pe.wait_ge(general_ready, 1)
            with pe.If(pe.value_load(general[0:1, 0:1], min_val=0, max_val=1) > 0):
                def step(n, entries, chunk):
                    pe.wait_ge(gen_turned_ready, n + 2)
                    pe.wait_ge(gen_weights_ready, n * 2 + 2)
                    pe.wait_ge(gen_added, n + 1)
                    nc.tensor.matmul(gen_ps[0:E, :], gen_weights, gen_turned,
                                     start=True, stop=True).then_inc(gen_multiplied, 1)
                gen_steps(pe.Fori, step)
                pe.wait_ge(row_ready, 1)
                finish(1)


_INS = ['r_x', 'L0_rec_V', 'L0_rec_bias', 'L0_rec_g_bias']
_OUTS = [((512, 1), 'float32')]


def kernel(**inputs):
    import numpy as _np
    import concourse.bacc as _bacc
    from concourse import mybir as _mybir
    from concourse.bass_utils import run_bass_kernel_spmd as _run

    nc = _bacc.Bacc("TRN2", target_bir_lowering=False, num_devices=1)
    arrays, args = {}, []
    for name in _INS:
        a = _np.ascontiguousarray(inputs[name])
        arrays[f"in_{name}_dram"] = a
        args.append(nc.dram_tensor(f"in_{name}_dram", a.shape, _mybir.dt.from_np(a.dtype), kind="ExternalInput").ap())
    for i, (shape, dtype) in enumerate(_OUTS):
        dt = _mybir.dt.from_np(_np.dtype(dtype))
        args.append(nc.dram_tensor(f"out_{i}_dram", shape, dt, kind="ExternalOutput").ap())
    factorization_machine(nc, *args)
    r = _run(nc, [arrays], core_ids=[0])
    got = tuple(r.results[0][f"out_{i}_dram"] for i in range(len(_OUTS)))
    return got[0]
```

```python
import concourse.bass as bass
from concourse import mybir
from contextlib import ExitStack


def factorization_machine(nc, x, V, bias, g_bias, out):
    fp32 = mybir.dt.float32
    bf16 = mybir.dt.bfloat16
    fp8 = mybir.dt.float8e4
    i32 = mybir.dt.int32
    u32 = mybir.dt.uint32
    ALU = mybir.AluOpType
    ACT = mybir.ActivationFunctionType
    AX = mybir.AxisListType

    B, K = x.shape
    F = V.shape[1]
    P = 128
    S = 32
    QUAD = 4
    W = QUAD * S
    NQ = P // S
    G = B // S
    NC = -(-K // P)
    ND = NC // QUAD
    Q = NC * S
    OVER = NQ * Q - K
    START = [i * Q for i in range(NQ - 1)] + [K - Q]
    assert NC == QUAD * ND + 1 and OVER < S
    E = F + 1

    NP = ND // 2
    HG = G // 2
    QG = G // 4
    LOWER, UPPER, THIRD, FOURTH = (0, HG), (HG, G), (HG, HG + QG), (HG + QG, G)
    LOADS = [(0, 2, *LOWER), (0, 2, *UPPER), (2, 6, *LOWER), (2, 6, *UPPER), (6, 10, *LOWER), (10, 12, *LOWER),
             (6, 10, *THIRD), (6, 10, *FOURTH), (10, 12, *THIRD), (10, 11, *FOURTH), (11, 12, *FOURTH)]
    UNITS = [(d, min(d + 2, d1), g0, g1) for d0, d1, g0, g1 in LOADS for d in range(d0, d1, 2)]
    LOAD_OF = [n for n, (d0, d1, g0, g1) in enumerate(LOADS) for d in range(d0, d1, 2)]
    NU = len(UNITS)
    PIECES = [LOWER, THIRD, FOURTH]
    LAST_OF_PIECE = [max(u for u, (d0, d1, g0, g1) in enumerate(UNITS) if g0 < p1 and p0 < g1) for p0, p1 in PIECES]
    V_LOADS = [(0, 1), (1, 2), (2, 4), (4, NP)]
    BEFORE_LOAD = [2, 3, 3, 4]
    V_LOAD_OF = [n for n, (a, b) in enumerate(V_LOADS) for _ in range(a, b)]
    BEFORE_CAST = [1, 2, 3, 3, 5, 6]
    BEFORE_TURN = [1, 2, 3, 3, 5, 7]
    LATE_CHECKS = 2
    FOLDED = G * S // 2
    FOLD_ODD, FOLD_HALF = 7, 8
    assert all((d1 - d0) * (g1 - g0) * S <= FOLDED for d0, d1, g0, g1 in UNITS[FOLD_HALF + 1:])
    NB = 4
    SHARED = [4, 6, 11, 12]
    assert ND % 2 == 0
    TOP_BITS = 0xC0C0C0C0
    TOP_BITS_ODD = 0xC000C000
    PARTS = 3

    def chunks(j):
        return (1 + 2 * QUAD * j if j else 0), 1 + 2 * QUAD * (j + 1)

    ctx = ExitStack()
    with ctx:
        def sb(name, shape, dt):
            return ctx.enter_context(nc.sbuf_tensor(name, shape, dt))

        def ps(name):
            return ctx.enter_context(nc.psum_tensor(name, [P, B], fp32))

        def sem(name):
            return ctx.enter_context(nc.semaphore(name))

        x_in = sb("x_in", [P, G, Q], i32)
        x_cast = [sb(f"x_cast{n}", [P, G * S], u32) for n in range(NB)]
        x_turned = [sb(f"x_turned{n}", [P, B], u32) for n in range(NB)]
        odd_cast = sb("odd_cast", [P, G, S], bf16)
        odd_turned = sb("odd_turned", [P, G, S], bf16)
        v_in = sb("v_in", [P, NC, F], fp32)
        v_rest = sb("v_rest", [P, NC, F], fp32)
        v_sq = sb("v_sq", [P, NC, F], fp32)
        upper = sb("upper", [P, NC, 2 * F], bf16)
        lower = sb("lower", [P, NC, F + PARTS + 1], bf16)
        bias_in = sb("bias_in", [P, W], fp32)
        bias_turned = sb("bias_turned", [P, QUAD, S], fp32)
        bias_odd = sb("bias_odd", [P, S], fp32)
        w_sum = sb("w_sum", [P, NC], fp32)
        w_all = sb("w_all", [P, NC], fp32)
        w_rest = sb("w_rest", [P, NC], fp32)
        H = F + PARTS + 1
        xv_mid = sb("xv_mid", [F, B], fp32)
        xv_low = sb("xv_low", [F, B], fp32)
        xv = sb("xv", [F, B], fp32)
        squares = sb("squares", [H, B], fp32)
        combine = sb("combine", [H, 1], fp32)
        ones = sb("ones", [P, 1], fp32)
        table_in = sb("table_in", [P, 1], fp32)
        MB = B // P
        y_sb = sb("y_sb", [P, MB], fp32)
        seen = sb("seen", [P, G * S], u32)
        odd_bits = sb("odd_bits", [P, G * S // 2], u32)
        foreign = sb("foreign", [P, 1], fp32)
        general = sb("general", [1, 1], i32)
        gen_float = x_cast[0][:, 0:B].bitcast(fp32).rearrange("p (g c) -> p g c", g=G)
        gen_turned = x_turned[0][:, :].bitcast(fp32)
        gen_weights = x_turned[2][:, 0:E].bitcast(fp32)
        gen_sum = x_turned[1][0:E, :].bitcast(fp32)
        upper_ps = [ps(f"upper_ps{k}") for k in range(len(PIECES))]
        lower_ps = [ps(f"lower_ps{k}") for k in range(len(PIECES))]
        y_ps = ps("y_ps")
        foreign_ps = y_ps[:, MB:MB + 1]
        gen_ps = ps("gen_ps")

        x_landed = [sem(f"x_landed{n}") for n in range(len(LOADS))]
        v_landed = [sem(f"v_landed{n}") for n in range(len(V_LOADS))]
        bias_landed = sem("bias_landed")
        g_landed = sem("g_landed")
        bias_cleared = sem("bias_cleared")
        overlap_cleared = sem("overlap_cleared")
        consts_set = sem("consts_set")
        table_loaded = sem("table_loaded")
        high_ready = sem("high_ready")
        v_squared = sem("v_squared")
        v_summed = sem("v_summed")
        v_split = sem("v_split")
        w_split = sem("w_split")
        rest_ready = sem("rest_ready")
        mid_ready = sem("mid_ready")
        mid_copied = sem("mid_copied")
        low_added = sem("low_added")
        xv_ready = sem("xv_ready")
        linear_cleared = sem("linear_cleared")
        x_cast_ready = sem("x_cast_ready")
        x_turned_ready = sem("x_turned_ready")
        odd_turned_ready = sem("odd_turned_ready")
        bias_turned_ready = sem("bias_turned_ready")
        w_odd = sem("w_odd")
        w_step = sem("w_step")
        bias_doubled = sem("bias_doubled")
        odd_cast_ready = sem("odd_cast_ready")
        x_seen = sem("x_seen")
        x_half_cast = sem("x_half_cast")
        odd_seen = sem("odd_seen")
        seen_folded = sem("seen_folded")
        masked = sem("masked")
        multiplied = sem("multiplied")
        squares_ready = sem("squares_ready")
        linear_ready = sem("linear_ready")
        y_ready = sem("y_ready")
        y_copied = sem("y_copied")
        foreign_ready = sem("foreign_ready")
        foreign_summed = sem("foreign_summed")
        general_ready = sem("general_ready")
        out_done = sem("out_done")
        gen_float_ready = sem("gen_float_ready")
        gen_turned_ready = sem("gen_turned_ready")
        gen_weights_ready = sem("gen_weights_ready")
        gen_multiplied = sem("gen_multiplied")
        gen_added = sem("gen_added")

        v_loads = [NQ + (2 if n == 0 else 0) for n in range(len(V_LOADS))]

        def load_v(queue, n):
            d0, d1 = (2 * j for j in V_LOADS[n])
            if n == 0:
                first = S * (NQ - 1)
                queue.dma_start(v_in[0:first, 0, :],
                                V[0:Q * (NQ - 1), :].rearrange("(i l) f -> i l f", l=Q)[:, 0:S, :]
                                ).then_inc(v_landed[0], 16)
                queue.dma_start(v_in[first:P, 0, :], V[START[NQ - 1]:START[NQ - 1] + S, :]).then_inc(v_landed[0], 16)
            for i in range(NQ):
                queue.dma_start(
                    v_in[S * i:S * i + S, 1 + QUAD * d0:1 + QUAD * d1, :].rearrange("c (d q) f -> c d (q f)", q=QUAD),
                    V[START[i] + S + d0 * W:START[i] + S + d1 * W, :].rearrange("(d c q) f -> c d (q f)", c=S, q=QUAD)
                ).then_inc(v_landed[n], 16)

        def load_x(queue, n):
            d0, d1, g0, g1 = LOADS[n]
            lo = S + d0 * W if d0 else 0
            hi = S + d1 * W
            for i in range(NQ):
                queue.dma_start(x_in[S * i:S * i + S, g0:g1, lo:hi],
                                x[g0 * S:g1 * S, START[i] + lo:START[i] + hi].rearrange("(g r) l -> r g l", r=S)
                                ).then_inc(x_landed[n], 16)

        def cast_operands(u, k0, k1):
            d0, d1, g0, g1 = UNITS[u]
            return (x_cast[u % NB][:, 0:words_of(u)].rearrange("p (g c) -> p g c", c=(d1 - d0) * S)[:, k0:k1],
                    x_in[:, g0 + k0:g0 + k1, S + d0 * W:S + d1 * W])

        def turn_operands(u, k0, k1):
            d0, d1, g0, g1 = UNITS[u]
            words = words_of(u)
            return (x_turned[u % NB][:, 0:words].rearrange("p (d g r) -> p d g r", d=d1 - d0, r=S)[:, :, k0:k1],
                    x_cast[u % NB][:, 0:words].rearrange("p (g d c) -> p d g c", d=d1 - d0, c=S)[:, :, k0:k1])

        def groups_of(u):
            d0, d1, g0, g1 = UNITS[u]
            return g1 - g0

        def words_of(u):
            d0, d1, g0, g1 = UNITS[u]
            return (d1 - d0) * (g1 - g0) * S

        def turned_by(u):
            return u + 1 + sum(v <= u for v in SHARED)

        def gen_steps(loop, step):
            with loop(0, ND) as d:
                for q in range(QUAD):
                    step(d * QUAD + q, x_in[:, :, bass.ds(d * W + S, W)].rearrange("p g (c q) -> p q g c", q=QUAD)[:, q],
                         d * QUAD + (q + 1))
            step(NC - 1, x_in[:, :, 0:S], 0)

        block = ctx.enter_context(nc.Block())

        @block.sync
        def _(sp):
            for n in range(len(LOADS)):
                for k in range(len(V_LOADS)):
                    if BEFORE_LOAD[k] == n:
                        load_v(sp, k)
                load_x(sp, n)

            y_out = out.rearrange("(p m) o -> p (m o)", m=MB)
            sp.wait_ge(y_copied, 1)
            sp.dma_start(y_out, y_sb[:, :]).then_inc(out_done, 16)
            sp.wait_ge(out_done, 16)
            sp.wait_ge(general_ready, 1)
            with sp.If(sp.value_load(general[0:1, 0:1], min_val=0, max_val=1) > 0):
                sp.wait_ge(y_copied, 2)
                sp.dma_start(y_out, y_sb[:, :]).then_inc(out_done, 16)
                sp.wait_ge(out_done, 32)

        @block.gpsimd
        def _(pool):
            nc.gpsimd.memset(bias_in[:, :], 0.0).then_inc(bias_cleared, 1)
            pool.wait_ge(bias_cleared, 1)
            pool.dma_start(bias_in[0:1, W - S:W], bias[0:S, :].rearrange("l o -> o l")).then_inc(bias_landed, 16)
            pool.dma_start(bias_in[1:1 + ND, :], bias[S:Q, :].rearrange("(d l) o -> d (l o)", l=W)
                           ).then_inc(bias_landed, 16)
            for i in range(1, NQ):
                pool.dma_start(bias_in[S * i:S * i + 1 + ND, :],
                               bias[START[i] + S - W:START[i] + Q, :].rearrange("(d l) o -> d (l o)", l=W)
                               ).then_inc(bias_landed, 16)
            pool.wait_ge(consts_set, 3)
            pool.dma_start(combine[H - 1:H, :], g_bias.rearrange("(a b) -> a b", b=1)).then_inc(g_landed, 16)
            last_quarter = S * (NQ - 1)
            pool.wait_ge(v_landed[0], 16 * v_loads[0])
            nc.gpsimd.memset(v_in[last_quarter:last_quarter + OVER, 0, :], 0.0).then_inc(overlap_cleared, 1)
            pool.wait_ge(bias_landed, 16 * (NQ + 1))
            pool.wait_ge(overlap_cleared, 1)
            nc.gpsimd.memset(bias_in[last_quarter:last_quarter + 1, W - S:W - S + OVER], 0.0
                             ).then_inc(overlap_cleared, 1)
            pool.wait_ge(overlap_cleared, 2)
            def remainder(n):
                a, b = chunks(n)
                pool.wait_ge(high_ready, n + 1)
                nc.gpsimd.tensor_tensor(v_rest[:, a:b, :], v_in[:, a:b, :], upper[:, a:b, 0:F], ALU.subtract
                                        ).then_inc(rest_ready, 1)

            def weigh(n):
                a, b = chunks(n)
                d0, d1 = 2 * n, 2 * n + 2
                high, mid, low = (lower[:, a:b, F + k] for k in range(PARTS))
                pool.wait_ge(v_summed, n + 1)
                if n == 0:
                    pool.wait_ge(bias_doubled, 2)
                    nc.gpsimd.tensor_tensor(w_all[:, 0:1], bias_odd[:, 0:1], w_sum[:, 0:1], ALU.subtract
                                            ).then_inc(w_odd, 1)
                    pool.wait_ge(w_odd, 1)
                quad_sums = slice(1 + QUAD * d0, 1 + QUAD * d1)
                nc.gpsimd.tensor_tensor(w_all[:, quad_sums].rearrange("p (d q) -> p d q", q=QUAD),
                                        bias_turned[:, :, 1 + d0:1 + d1].rearrange("p q d -> p d q"),
                                        w_sum[:, quad_sums].rearrange("p (d q) -> p d q", q=QUAD),
                                        ALU.subtract).then_inc(w_step, 1)
                pool.wait_ge(w_step, 4 * n + 1)
                nc.gpsimd.tensor_copy(high, w_all[:, a:b]).then_inc(w_step, 1)
                pool.wait_ge(w_step, 4 * n + 2)
                nc.gpsimd.tensor_tensor(w_rest[:, a:b], w_all[:, a:b], high, ALU.subtract).then_inc(w_step, 1)
                pool.wait_ge(w_step, 4 * n + 3)
                nc.gpsimd.tensor_copy(mid, w_rest[:, a:b]).then_inc(w_step, 1)
                pool.wait_ge(w_step, 4 * n + 4)
                nc.gpsimd.tensor_tensor(low, w_rest[:, a:b], mid, ALU.subtract).then_inc(w_split, 1)
                pool.wait_ge(w_split, n + 1)

            for n in range(NP):
                remainder(n)
                weigh(n)

        @block.scalar
        def _(act):
            def prepare(n):
                a, b = chunks(n)
                load = V_LOAD_OF[n]
                act.wait_ge(v_landed[load], 16 * v_loads[load])
                if n == 0:
                    act.wait_ge(overlap_cleared, 1)
                nc.scalar.copy(upper[:, a:b, 0:F], v_in[:, a:b, :]).then_inc(high_ready, 1)
                nc.scalar.activation(v_sq[:, a:b, :], v_in[:, a:b, :], ACT.Square).then_inc(v_squared, 1)

            def cast(u):
                act.wait_ge(x_landed[LOAD_OF[u]], 16 * NQ)
                if u >= NB:
                    act.wait_ge(x_seen, u - NB + 1)
                words, entries = cast_operands(u, 0, groups_of(u) // 2 if u in SHARED else groups_of(u))
                nc.scalar.copy(words.bitcast(fp8), entries, saturate=False).then_inc(x_cast_ready, 1)

            act.wait_ge(consts_set, 3)
            nc.scalar.activation(table_in[:, :], ones[:, :], ACT.Square).then_inc(table_loaded, 1)
            for u in range(NU):
                for n in range(NP):
                    if BEFORE_CAST[n] == u:
                        prepare(n)
                cast(u)

            def copy_sums(k):
                p0, p1 = PIECES[k]
                rows, N = slice(p0 * S, p1 * S), (p1 - p0) * S
                act.wait_ge(multiplied, LAST_OF_PIECE[k] + 1)
                nc.scalar.copy(xv_mid[:, rows], upper_ps[k][F:2 * F, 0:N]).then_inc(mid_copied, 1)
                nc.scalar.copy(squares[F:F + PARTS, rows], lower_ps[k][F:F + PARTS, 0:N]).then_inc(linear_ready, 1)

            def square(k):
                p0, p1 = PIECES[k]
                rows = slice(p0 * S, p1 * S)
                act.wait_ge(xv_ready, k + 1)
                nc.scalar.activation(squares[0:F, rows], xv[:, rows], ACT.Square).then_inc(squares_ready, 1)

            copy_sums(0)
            copy_sums(1)
            square(0)
            copy_sums(2)
            square(1)
            square(2)
            act.wait_ge(general_ready, 1)
            with act.If(act.value_load(general[0:1, 0:1], min_val=0, max_val=1) > 0):
                def step(n, entries, chunk):
                    act.wait_ge(gen_turned_ready, n + 1)
                    nc.scalar.copy(gen_float, entries).then_inc(gen_float_ready, 1)
                gen_steps(act.Fori, step)
                act.wait_ge(gen_added, NC + 1)
                act.wait_ge(y_ready, MB * len(PIECES))
                nc.scalar.activation(squares[0:F, :], gen_sum[0:F, :], ACT.Square).then_inc(squares_ready, 1)

        @block.vector
        def _(dve):
            nc.vector.memset(combine[:, :], 0.5).then_inc(consts_set, 1)
            nc.vector.memset(ones[:, :], 1.0).then_inc(consts_set, 1)
            nc.vector.memset(squares[F:H, :], 1.0).then_inc(consts_set, 1)

            def turn_odd(h):
                groups = slice(h * HG, (h + 1) * HG)
                dve.wait_ge(x_landed[h], 16 * NQ)
                nc.vector.tensor_copy(odd_cast[:, groups, :], x_in[:, groups, 0:S]).then_inc(odd_cast_ready, 1)
                dve.wait_ge(odd_cast_ready, h + 1)
                nc.vector.transpose(odd_turned[:, groups, :], odd_cast[:, groups, :]).then_inc(odd_turned_ready, 1)

            def turn(u):
                groups = groups_of(u)
                steps = [(0, groups)]
                if u in SHARED:
                    dve.wait_ge(x_landed[LOAD_OF[u]], 16 * NQ)
                    dve.wait_ge(x_seen, u - NB + 1)
                    words, entries = cast_operands(u, groups // 2, groups)
                    nc.vector.tensor_copy(words.bitcast(fp8), entries, saturate=False).then_inc(x_half_cast, 1)
                    dve.wait_ge(x_half_cast, SHARED.index(u) + 1)
                    steps = [(groups // 2, groups), (0, groups // 2)]
                if u >= NB:
                    dve.wait_ge(multiplied, u - NB + 1)
                for k0, k1 in steps:
                    if k0 == 0:
                        dve.wait_ge(x_cast_ready, u + 1)
                    turned, words = turn_operands(u, k0, k1)
                    nc.vector.transpose(turned, words).then_inc(x_turned_ready, 1)

            def check(u):
                if u == 0:
                    nc.vector.tensor_copy(seen[:, :], x_cast[0][:, :]).then_inc(x_seen, 1)
                    return
                dve.wait_ge(x_seen, u)
                if u > FOLD_ODD:
                    dve.wait_ge(seen_folded, 1 + (u > FOLD_HALF))
                words = words_of(u)
                nc.vector.tensor_tensor(seen[:, 0:words], seen[:, 0:words], x_cast[u % NB][:, 0:words],
                                        ALU.bitwise_or).then_inc(x_seen, 1)

            def fold(u, bits):
                dve.wait_ge(x_seen, u + 1)
                nc.vector.tensor_tensor(seen[:, 0:FOLDED], seen[:, 0:FOLDED], bits, ALU.bitwise_or
                                        ).then_inc(seen_folded, 1)

            def add_parts(k):
                p0, p1 = PIECES[k]
                rows, N = slice(p0 * S, p1 * S), (p1 - p0) * S
                dve.wait_ge(mid_copied, k + 1)
                nc.vector.tensor_tensor(xv_low[:, rows], xv_mid[:, rows], lower_ps[k][0:F, 0:N], ALU.add
                                        ).then_inc(low_added, 1)
                dve.wait_ge(low_added, k + 1)
                nc.vector.tensor_tensor(xv[:, rows], xv_low[:, rows], upper_ps[k][0:F, 0:N], ALU.add
                                        ).then_inc(xv_ready, 1)

            def prepare(n):
                a, b = chunks(n)
                rest = v_rest[:, a:b, :]
                mid, low = upper[:, a:b, F:2 * F], lower[:, a:b, 0:F]
                dve.wait_ge(v_squared, n + 1)
                nc.vector.tensor_reduce(w_sum[:, a:b], v_sq[:, a:b, :], AX.X, ALU.add).then_inc(v_summed, 1)
                dve.wait_ge(rest_ready, n + 1)
                nc.vector.tensor_copy(mid, rest).then_inc(mid_ready, 1)
                dve.wait_ge(mid_ready, n + 1)
                nc.vector.tensor_tensor(low, rest, mid, ALU.subtract).then_inc(v_split, 1)

            turn_odd(0)
            dve.wait_ge(bias_landed, 16 * (NQ + 1))
            dve.wait_ge(overlap_cleared, 2)
            nc.vector.transpose(bias_odd[:, :], bias_in[:, W - S:W]).then_inc(bias_turned_ready, 1)
            nc.vector.transpose(bias_turned[:, :, :], bias_in[:, :].rearrange("p (c q) -> p q c", q=QUAD)
                                ).then_inc(bias_turned_ready, 1)
            dve.wait_ge(bias_turned_ready, 2)
            for turned in (bias_odd[:, :], bias_turned[:, :, :]):
                nc.vector.tensor_scalar(turned, turned, 2.0, None, ALU.mult).then_inc(bias_doubled, 1)
            for u in range(NU):
                for n in range(NP):
                    if BEFORE_TURN[n] == u:
                        prepare(n)
                if u == 1:
                    turn_odd(1)
                    nc.vector.tensor_scalar(odd_bits[:, :], odd_cast[:, :, :].rearrange("p g l -> p (g l)").bitcast(u32),
                                            TOP_BITS_ODD, None, ALU.bitwise_and).then_inc(odd_seen, 1)
                turn(u)
                if u < NU - LATE_CHECKS:
                    check(u)
                if u == FOLD_ODD:
                    dve.wait_ge(odd_seen, 1)
                    fold(u, odd_bits[:, :])
                if u == FOLD_HALF:
                    fold(u, seen[:, FOLDED:])
            for k in range(len(PIECES)):
                add_parts(k)
            for u in range(NU - LATE_CHECKS, NU):
                check(u)

            def finish(n):
                dve.wait_ge(y_ready, MB * len(PIECES) * (n + 1))
                nc.vector.tensor_copy(y_sb[:, :], y_ps[:, 0:MB]).then_inc(y_copied, 1)

            finish(0)
            dve.wait_ge(x_seen, NU)
            nc.vector.tensor_scalar(seen[:, 0:FOLDED], seen[:, 0:FOLDED], TOP_BITS, None, ALU.bitwise_and
                                    ).then_inc(masked, 1)
            dve.wait_ge(masked, 1)
            nc.vector.tensor_reduce(foreign[:, :], seen[:, 0:FOLDED], AX.X, ALU.max).then_inc(foreign_ready, 1)
            dve.wait_ge(foreign_summed, 1)
            nc.vector.tensor_scalar(general[0:1, 0:1], foreign_ps[0:1, 0:1], 0.0, None, ALU.is_gt).then_inc(general_ready, 1)
            dve.wait_ge(general_ready, 1)
            with dve.If(dve.value_load(general[0:1, 0:1], min_val=0, max_val=1) > 0):
                dve.sem_inc(gen_turned_ready, 1)
                nc.vector.memset(gen_sum, 0.0).then_inc(gen_added, 1)
                dve.wait_ge(gen_added, 1)

                def step(n, entries, chunk):
                    dve.wait_ge(gen_float_ready, n + 1)
                    nc.vector.transpose(gen_turned.rearrange("p (g r) -> p g r", g=G),
                                        gen_float).then_inc(gen_turned_ready, 1)
                    nc.vector.tensor_copy(gen_weights[:, 0:F], v_in[:, bass.ds(chunk, 1), :].rearrange("p n f -> p (n f)")
                                          ).then_inc(gen_weights_ready, 1)
                    nc.vector.tensor_copy(gen_weights[:, F:E], w_all[:, bass.ds(chunk, 1)]).then_inc(gen_weights_ready, 1)
                    dve.wait_ge(gen_multiplied, n + 1)
                    nc.vector.tensor_tensor(gen_sum, gen_sum, gen_ps[0:E, :], ALU.add
                                            ).then_inc(gen_added, 1)
                    dve.wait_ge(gen_added, n + 2)
                gen_steps(dve.Fori, step)
                nc.vector.memset(squares[F:F + PARTS, :], 0.0).then_inc(linear_cleared, 1)
                dve.wait_ge(linear_cleared, 1)
                nc.vector.tensor_copy(squares[F:E, :], gen_sum[F:E, :]).then_inc(linear_ready, 1)
                dve.wait_ge(out_done, 16)
                finish(1)

        @block.tensor
        def _(pe):
            for u in range(NU):
                d0, d1, g0, g1 = UNITS[u]
                if g0 == 0:
                    pe.wait_ge(v_split, d1 // 2)
                    pe.wait_ge(w_split, d1 // 2)
                pe.wait_ge(x_turned_ready, turned_by(u))
                entries = x_turned[u % NB][:, 0:words_of(u)].bitcast(fp8).rearrange("p (d b q) -> p d q b", d=d1 - d0, q=QUAD)
                moving = [entries[:, d, q, :] for d in range(d1 - d0) for q in range(QUAD)]
                if d0 == 0:
                    pe.wait_ge(odd_turned_ready, u + 1)
                    moving.insert(0, odd_turned[:, g0:g1, :].rearrange("p g r -> p (g r)"))
                pieces = [(k, p0, p1) for k, (p0, p1) in enumerate(PIECES) if g0 < p1 and p0 < g1]
                for n, column in enumerate(moving, 1 + QUAD * d0 if d0 else 0):
                    for k, p0, p1 in pieces:
                        lo, hi = max(g0, p0), min(g1, p1)
                        for weights, sums in ((upper[:, n, :], upper_ps[k]), (lower[:, n, 0:F + PARTS], lower_ps[k])):
                            last = nc.tensor.matmul(sums[0:weights.shape[1], (lo - p0) * S:(hi - p0) * S], weights,
                                                    column[:, (lo - g0) * S:(hi - g0) * S],
                                                    start=(n == 0), stop=(u == LAST_OF_PIECE[k] and n == NC - 1))
                last.then_inc(multiplied, 1)

            def finish(k, ready):
                rows = squares[:, :].rearrange("f (p m) -> f m p", m=MB)
                pe.wait_ge(squares_ready, ready)
                pe.wait_ge(linear_ready, ready)
                p0, p1 = PIECES[k]
                part = slice(p0 * S // MB, p1 * S // MB)
                for m in range(MB):
                    nc.tensor.matmul(y_ps[part, m:m + 1], rows[:, m, part], combine[:, :], start=True, stop=True
                                     ).then_inc(y_ready, 1)

            pe.wait_ge(consts_set, 3)
            pe.wait_ge(g_landed, 16)
            for k in range(len(PIECES)):
                finish(k, k + 1)
            pe.wait_ge(foreign_ready, 1)
            nc.tensor.matmul(foreign_ps[0:1, 0:1], foreign[:, :], ones[:, :], start=True, stop=True
                             ).then_inc(foreign_summed, 1)
            pe.wait_ge(general_ready, 1)
            with pe.If(pe.value_load(general[0:1, 0:1], min_val=0, max_val=1) > 0):
                def step(n, entries, chunk):
                    pe.wait_ge(gen_turned_ready, n + 2)
                    pe.wait_ge(gen_weights_ready, n * 2 + 2)
                    pe.wait_ge(gen_added, n + 1)
                    nc.tensor.matmul(gen_ps[0:E, :], gen_weights, gen_turned,
                                     start=True, stop=True).then_inc(gen_multiplied, 1)
                gen_steps(pe.Fori, step)
                pe.wait_ge(y_copied, 1)
                for k in range(len(PIECES)):
                    finish(k, len(PIECES) + 1)


_INS = ['r_x', 'L0_rec_V', 'L0_rec_bias', 'L0_rec_g_bias']
_OUTS = [((512, 1), 'float32')]


def kernel(**inputs):
    import numpy as _np
    import concourse.bacc as _bacc
    from concourse import mybir as _mybir
    from concourse.bass_utils import run_bass_kernel_spmd as _run

    nc = _bacc.Bacc("TRN2", target_bir_lowering=False, num_devices=1)
    arrays, args = {}, []
    for name in _INS:
        a = _np.ascontiguousarray(inputs[name])
        arrays[f"in_{name}_dram"] = a
        args.append(nc.dram_tensor(f"in_{name}_dram", a.shape, _mybir.dt.from_np(a.dtype), kind="ExternalInput").ap())
    for i, (shape, dtype) in enumerate(_OUTS):
        dt = _mybir.dt.from_np(_np.dtype(dtype))
        args.append(nc.dram_tensor(f"out_{i}_dram", shape, dt, kind="ExternalOutput").ap())
    factorization_machine(nc, *args)
    r = _run(nc, [arrays], core_ids=[0])
    got = tuple(r.results[0][f"out_{i}_dram"] for i in range(len(_OUTS)))
    return got[0]
```
